# Optimizing a Trainium2 kernel written in Bass

```python
import numpy as np
import jax
import jax.numpy as jnp

def _softmax(x, axis=-1):
    return jax.nn.softmax(x, axis=axis)
def _gelu(x):
    return jax.nn.gelu(x, approximate=True)
def _silu(x):
    return jax.nn.silu(x)
def _sigmoid(x):
    return jax.nn.sigmoid(x)
def _layernorm(x, axis=-1, eps=1e-5):
    m = jnp.mean(x, axis=axis, keepdims=True)
    v = jnp.var(x, axis=axis, keepdims=True)
    return (x - m) / jnp.sqrt(v + eps)
def _scatter_add(tgt, idx, src, axis=0):
    return tgt.at[idx].add(src)
def _segment_sum(src, seg, n):
    return jax.ops.segment_sum(src, seg, n)

kernel_name = 'mk_rec_standalone_d1_rec_9c3e1a'

def setup_inputs(seed: int = 0):
    np.random.seed(seed)
    _w = jnp.asarray
    def _rec_inputs():
        import jax
        import jax.numpy as jnp
        _rk = jax.random.key(seed)
        r_x = jnp.stack([jax.random.randint(jax.random.fold_in(jax.random.fold_in(_rk, 1), 0), (16384,), 16, 99990, jnp.int32), jax.random.randint(jax.random.fold_in(jax.random.fold_in(_rk, 1), 1), (16384,), 4, 99979, jnp.int32), jax.random.randint(jax.random.fold_in(jax.random.fold_in(_rk, 1), 2), (16384,), 7, 99997, jnp.int32), jax.random.randint(jax.random.fold_in(jax.random.fold_in(_rk, 1), 3), (16384,), 72, 99991, jnp.int32), jax.random.randint(jax.random.fold_in(jax.random.fold_in(_rk, 1), 4), (16384,), 20, 99994, jnp.int32), jax.random.randint(jax.random.fold_in(jax.random.fold_in(_rk, 1), 5), (16384,), 22, 100001, jnp.int32), jax.random.randint(jax.random.fold_in(jax.random.fold_in(_rk, 1), 6), (16384,), 16, 99976, jnp.int32), jax.random.randint(jax.random.fold_in(jax.random.fold_in(_rk, 1), 7), (16384,), 10, 99997, jnp.int32), jax.random.randint(jax.random.fold_in(jax.random.fold_in(_rk, 1), 8), (16384,), 12, 99914, jnp.int32), jax.random.randint(jax.random.fold_in(jax.random.fold_in(_rk, 1), 9), (16384,), 101, 99973, jnp.int32), jax.random.randint(jax.random.fold_in(jax.random.fold_in(_rk, 1), 10), (16384,), 9, 99995, jnp.int32), jax.random.randint(jax.random.fold_in(jax.random.fold_in(_rk, 1), 11), (16384,), 7, 99998, jnp.int32), jax.random.randint(jax.random.fold_in(jax.random.fold_in(_rk, 1), 12), (16384,), 28, 99974, jnp.int32), jax.random.randint(jax.random.fold_in(jax.random.fold_in(_rk, 1), 13), (16384,), 1, 99923, jnp.int32), jax.random.randint(jax.random.fold_in(jax.random.fold_in(_rk, 1), 14), (16384,), 2, 99988, jnp.int32), jax.random.randint(jax.random.fold_in(jax.random.fold_in(_rk, 1), 15), (16384,), 6, 99931, jnp.int32), jax.random.randint(jax.random.fold_in(jax.random.fold_in(_rk, 1), 16), (16384,), 50, 99989, jnp.int32), jax.random.randint(jax.random.fold_in(jax.random.fold_in(_rk, 1), 17), (16384,), 10, 99983, jnp.int32), jax.random.randint(jax.random.fold_in(jax.random.fold_in(_rk, 1), 18), (16384,), 38, 100000, jnp.int32), jax.random.randint(jax.random.fold_in(jax.random.fold_in(_rk, 1), 19), (16384,), 10, 100000, jnp.int32), jax.random.randint(jax.random.fold_in(jax.random.fold_in(_rk, 1), 20), (16384,), 87, 100000, jnp.int32), jax.random.randint(jax.random.fold_in(jax.random.fold_in(_rk, 1), 21), (16384,), 21, 99987, jnp.int32), jax.random.randint(jax.random.fold_in(jax.random.fold_in(_rk, 1), 22), (16384,), 2, 99997, jnp.int32), jax.random.randint(jax.random.fold_in(jax.random.fold_in(_rk, 1), 23), (16384,), 2, 99976, jnp.int32), jax.random.randint(jax.random.fold_in(jax.random.fold_in(_rk, 1), 24), (16384,), 2, 99964, jnp.int32), jax.random.randint(jax.random.fold_in(jax.random.fold_in(_rk, 1), 25), (16384,), 30, 99998, jnp.int32), jax.random.randint(jax.random.fold_in(jax.random.fold_in(_rk, 1), 26), (16384,), 5, 99960, jnp.int32), jax.random.randint(jax.random.fold_in(jax.random.fold_in(_rk, 1), 27), (16384,), 16, 99965, jnp.int32), jax.random.randint(jax.random.fold_in(jax.random.fold_in(_rk, 1), 28), (16384,), 35, 99980, jnp.int32), jax.random.randint(jax.random.fold_in(jax.random.fold_in(_rk, 1), 29), (16384,), 29, 99972, jnp.int32), jax.random.randint(jax.random.fold_in(jax.random.fold_in(_rk, 1), 30), (16384,), 21, 99993, jnp.int32), jax.random.randint(jax.random.fold_in(jax.random.fold_in(_rk, 1), 31), (16384,), 0, 99924, jnp.int32), jax.random.randint(jax.random.fold_in(jax.random.fold_in(_rk, 1), 32), (16384,), 27, 99983, jnp.int32), jax.random.randint(jax.random.fold_in(jax.random.fold_in(_rk, 1), 33), (16384,), 5, 99999, jnp.int32), jax.random.randint(jax.random.fold_in(jax.random.fold_in(_rk, 1), 34), (16384,), 5, 99937, jnp.int32), jax.random.randint(jax.random.fold_in(jax.random.fold_in(_rk, 1), 35), (16384,), 78, 99985, jnp.int32), jax.random.randint(jax.random.fold_in(jax.random.fold_in(_rk, 1), 36), (16384,), 6, 99995, jnp.int32), jax.random.randint(jax.random.fold_in(jax.random.fold_in(_rk, 1), 37), (16384,), 11, 99959, jnp.int32), jax.random.randint(jax.random.fold_in(jax.random.fold_in(_rk, 1), 38), (16384,), 3, 99999, jnp.int32), jax.random.randint(jax.random.fold_in(jax.random.fold_in(_rk, 1), 39), (16384,), 32, 99999, jnp.int32), jax.random.randint(jax.random.fold_in(jax.random.fold_in(_rk, 1), 40), (16384,), 30, 99993, jnp.int32), jax.random.randint(jax.random.fold_in(jax.random.fold_in(_rk, 1), 41), (16384,), 62, 99977, jnp.int32), jax.random.randint(jax.random.fold_in(jax.random.fold_in(_rk, 1), 42), (16384,), 10, 99995, jnp.int32), jax.random.randint(jax.random.fold_in(jax.random.fold_in(_rk, 1), 43), (16384,), 0, 99984, jnp.int32), jax.random.randint(jax.random.fold_in(jax.random.fold_in(_rk, 1), 44), (16384,), 2, 99996, jnp.int32), jax.random.randint(jax.random.fold_in(jax.random.fold_in(_rk, 1), 45), (16384,), 10, 99975, jnp.int32), jax.random.randint(jax.random.fold_in(jax.random.fold_in(_rk, 1), 46), (16384,), 1, 99974, jnp.int32), jax.random.randint(jax.random.fold_in(jax.random.fold_in(_rk, 1), 47), (16384,), 105, 99984, jnp.int32), jax.random.randint(jax.random.fold_in(jax.random.fold_in(_rk, 1), 48), (16384,), 2, 100000, jnp.int32), jax.random.randint(jax.random.fold_in(jax.random.fold_in(_rk, 1), 49), (16384,), 7, 99982, jnp.int32), jax.random.randint(jax.random.fold_in(jax.random.fold_in(_rk, 1), 50), (16384,), 35, 99974, jnp.int32), jax.random.randint(jax.random.fold_in(jax.random.fold_in(_rk, 1), 51), (16384,), 44, 99996, jnp.int32), jax.random.randint(jax.random.fold_in(jax.random.fold_in(_rk, 1), 52), (16384,), 35, 99988, jnp.int32), jax.random.randint(jax.random.fold_in(jax.random.fold_in(_rk, 1), 53), (16384,), 1, 99883, jnp.int32), jax.random.randint(jax.random.fold_in(jax.random.fold_in(_rk, 1), 54), (16384,), 30, 99980, jnp.int32), jax.random.randint(jax.random.fold_in(jax.random.fold_in(_rk, 1), 55), (16384,), 21, 99853, jnp.int32), jax.random.randint(jax.random.fold_in(jax.random.fold_in(_rk, 1), 56), (16384,), 49, 99948, jnp.int32), jax.random.randint(jax.random.fold_in(jax.random.fold_in(_rk, 1), 57), (16384,), 39, 99987, jnp.int32), jax.random.randint(jax.random.fold_in(jax.random.fold_in(_rk, 1), 58), (16384,), 11, 99998, jnp.int32), jax.random.randint(jax.random.fold_in(jax.random.fold_in(_rk, 1), 59), (16384,), 51, 99968, jnp.int32), jax.random.randint(jax.random.fold_in(jax.random.fold_in(_rk, 1), 60), (16384,), 32, 99813, jnp.int32), jax.random.randint(jax.random.fold_in(jax.random.fold_in(_rk, 1), 61), (16384,), 14, 99972, jnp.int32), jax.random.randint(jax.random.fold_in(jax.random.fold_in(_rk, 1), 62), (16384,), 15, 100001, jnp.int32), jax.random.randint(jax.random.fold_in(jax.random.fold_in(_rk, 1), 63), (16384,), 5, 99991, jnp.int32), jax.random.randint(jax.random.fold_in(jax.random.fold_in(_rk, 1), 64), (16384,), 35, 99956, jnp.int32), jax.random.randint(jax.random.fold_in(jax.random.fold_in(_rk, 1), 65), (16384,), 34, 99970, jnp.int32), jax.random.randint(jax.random.fold_in(jax.random.fold_in(_rk, 1), 66), (16384,), 21, 99988, jnp.int32), jax.random.randint(jax.random.fold_in(jax.random.fold_in(_rk, 1), 67), (16384,), 22, 99993, jnp.int32), jax.random.randint(jax.random.fold_in(jax.random.fold_in(_rk, 1), 68), (16384,), 44, 99946, jnp.int32), jax.random.randint(jax.random.fold_in(jax.random.fold_in(_rk, 1), 69), (16384,), 41, 99997, jnp.int32), jax.random.randint(jax.random.fold_in(jax.random.fold_in(_rk, 1), 70), (16384,), 37, 99932, jnp.int32), jax.random.randint(jax.random.fold_in(jax.random.fold_in(_rk, 1), 71), (16384,), 29, 99969, jnp.int32), jax.random.randint(jax.random.fold_in(jax.random.fold_in(_rk, 1), 72), (16384,), 5, 99997, jnp.int32), jax.random.randint(jax.random.fold_in(jax.random.fold_in(_rk, 1), 73), (16384,), 3, 99990, jnp.int32), jax.random.randint(jax.random.fold_in(jax.random.fold_in(_rk, 1), 74), (16384,), 30, 99950, jnp.int32), jax.random.randint(jax.random.fold_in(jax.random.fold_in(_rk, 1), 75), (16384,), 29, 99988, jnp.int32), jax.random.randint(jax.random.fold_in(jax.random.fold_in(_rk, 1), 76), (16384,), 25, 99984, jnp.int32), jax.random.randint(jax.random.fold_in(jax.random.fold_in(_rk, 1), 77), (16384,), 9, 99954, jnp.int32), jax.random.randint(jax.random.fold_in(jax.random.fold_in(_rk, 1), 78), (16384,), 15, 99951, jnp.int32), jax.random.randint(jax.random.fold_in(jax.random.fold_in(_rk, 1), 79), (16384,), 8, 99995, jnp.int32), jax.random.randint(jax.random.fold_in(jax.random.fold_in(_rk, 1), 80), (16384,), 50, 99999, jnp.int32), jax.random.randint(jax.random.fold_in(jax.random.fold_in(_rk, 1), 81), (16384,), 5, 99991, jnp.int32), jax.random.randint(jax.random.fold_in(jax.random.fold_in(_rk, 1), 82), (16384,), 14, 99993, jnp.int32), jax.random.randint(jax.random.fold_in(jax.random.fold_in(_rk, 1), 83), (16384,), 9, 99937, jnp.int32), jax.random.randint(jax.random.fold_in(jax.random.fold_in(_rk, 1), 84), (16384,), 2, 99966, jnp.int32), jax.random.randint(jax.random.fold_in(jax.random.fold_in(_rk, 1), 85), (16384,), 150, 99987, jnp.int32), jax.random.randint(jax.random.fold_in(jax.random.fold_in(_rk, 1), 86), (16384,), 21, 99809, jnp.int32), jax.random.randint(jax.random.fold_in(jax.random.fold_in(_rk, 1), 87), (16384,), 10, 99997, jnp.int32), jax.random.randint(jax.random.fold_in(jax.random.fold_in(_rk, 1), 88), (16384,), 10, 99928, jnp.int32), jax.random.randint(jax.random.fold_in(jax.random.fold_in(_rk, 1), 89), (16384,), 3, 99993, jnp.int32), jax.random.randint(jax.random.fold_in(jax.random.fold_in(_rk, 1), 90), (16384,), 57, 99987, jnp.int32), jax.random.randint(jax.random.fold_in(jax.random.fold_in(_rk, 1), 91), (16384,), 19, 99982, jnp.int32), jax.random.randint(jax.random.fold_in(jax.random.fold_in(_rk, 1), 92), (16384,), 29, 99985, jnp.int32), jax.random.randint(jax.random.fold_in(jax.random.fold_in(_rk, 1), 93), (16384,), 6, 99975, jnp.int32), jax.random.randint(jax.random.fold_in(jax.random.fold_in(_rk, 1), 94), (16384,), 7, 99985, jnp.int32), jax.random.randint(jax.random.fold_in(jax.random.fold_in(_rk, 1), 95), (16384,), 47, 99998, jnp.int32), jax.random.randint(jax.random.fold_in(jax.random.fold_in(_rk, 1), 96), (16384,), 32, 99979, jnp.int32), jax.random.randint(jax.random.fold_in(jax.random.fold_in(_rk, 1), 97), (16384,), 6, 100000, jnp.int32), jax.random.randint(jax.random.fold_in(jax.random.fold_in(_rk, 1), 98), (16384,), 11, 99991, jnp.int32), jax.random.randint(jax.random.fold_in(jax.random.fold_in(_rk, 1), 99), (16384,), 39, 99997, jnp.int32), jax.random.randint(jax.random.fold_in(jax.random.fold_in(_rk, 1), 100), (16384,), 15, 99994, jnp.int32), jax.random.randint(jax.random.fold_in(jax.random.fold_in(_rk, 1), 101), (16384,), 15, 99990, jnp.int32), jax.random.randint(jax.random.fold_in(jax.random.fold_in(_rk, 1), 102), (16384,), 45, 99996, jnp.int32), jax.random.randint(jax.random.fold_in(jax.random.fold_in(_rk, 1), 103), (16384,), 15, 99962, jnp.int32), jax.random.randint(jax.random.fold_in(jax.random.fold_in(_rk, 1), 104), (16384,), 8, 99982, jnp.int32), jax.random.randint(jax.random.fold_in(jax.random.fold_in(_rk, 1), 105), (16384,), 9, 99996, jnp.int32), jax.random.randint(jax.random.fold_in(jax.random.fold_in(_rk, 1), 106), (16384,), 5, 99946, jnp.int32), jax.random.randint(jax.random.fold_in(jax.random.fold_in(_rk, 1), 107), (16384,), 16, 99983, jnp.int32), jax.random.randint(jax.random.fold_in(jax.random.fold_in(_rk, 1), 108), (16384,), 10, 99979, jnp.int32), jax.random.randint(jax.random.fold_in(jax.random.fold_in(_rk, 1), 109), (16384,), 28, 99916, jnp.int32), jax.random.randint(jax.random.fold_in(jax.random.fold_in(_rk, 1), 110), (16384,), 12, 99995, jnp.int32), jax.random.randint(jax.random.fold_in(jax.random.fold_in(_rk, 1), 111), (16384,), 38, 99976, jnp.int32), jax.random.randint(jax.random.fold_in(jax.random.fold_in(_rk, 1), 112), (16384,), 3, 99999, jnp.int32), jax.random.randint(jax.random.fold_in(jax.random.fold_in(_rk, 1), 113), (16384,), 56, 99935, jnp.int32), jax.random.randint(jax.random.fold_in(jax.random.fold_in(_rk, 1), 114), (16384,), 43, 99975, jnp.int32), jax.random.randint(jax.random.fold_in(jax.random.fold_in(_rk, 1), 115), (16384,), 7, 99989, jnp.int32), jax.random.randint(jax.random.fold_in(jax.random.fold_in(_rk, 1), 116), (16384,), 18, 99959, jnp.int32), jax.random.randint(jax.random.fold_in(jax.random.fold_in(_rk, 1), 117), (16384,), 1, 99968, jnp.int32), jax.random.randint(jax.random.fold_in(jax.random.fold_in(_rk, 1), 118), (16384,), 10, 99988, jnp.int32), jax.random.randint(jax.random.fold_in(jax.random.fold_in(_rk, 1), 119), (16384,), 44, 100000, jnp.int32), jax.random.randint(jax.random.fold_in(jax.random.fold_in(_rk, 1), 120), (16384,), 21, 99994, jnp.int32), jax.random.randint(jax.random.fold_in(jax.random.fold_in(_rk, 1), 121), (16384,), 2, 99975, jnp.int32), jax.random.randint(jax.random.fold_in(jax.random.fold_in(_rk, 1), 122), (16384,), 40, 99990, jnp.int32), jax.random.randint(jax.random.fold_in(jax.random.fold_in(_rk, 1), 123), (16384,), 32, 99995, jnp.int32), jax.random.randint(jax.random.fold_in(jax.random.fold_in(_rk, 1), 124), (16384,), 21, 99989, jnp.int32), jax.random.randint(jax.random.fold_in(jax.random.fold_in(_rk, 1), 125), (16384,), 19, 99979, jnp.int32), jax.random.randint(jax.random.fold_in(jax.random.fold_in(_rk, 1), 126), (16384,), 0, 99990, jnp.int32), jax.random.randint(jax.random.fold_in(jax.random.fold_in(_rk, 1), 127), (16384,), 5, 99992, jnp.int32), jax.random.randint(jax.random.fold_in(jax.random.fold_in(_rk, 1), 128), (16384,), 2, 99982, jnp.int32), jax.random.randint(jax.random.fold_in(jax.random.fold_in(_rk, 1), 129), (16384,), 0, 99975, jnp.int32), jax.random.randint(jax.random.fold_in(jax.random.fold_in(_rk, 1), 130), (16384,), 29, 99992, jnp.int32), jax.random.randint(jax.random.fold_in(jax.random.fold_in(_rk, 1), 131), (16384,), 7, 99949, jnp.int32), jax.random.randint(jax.random.fold_in(jax.random.fold_in(_rk, 1), 132), (16384,), 9, 99990, jnp.int32), jax.random.randint(jax.random.fold_in(jax.random.fold_in(_rk, 1), 133), (16384,), 97, 99991, jnp.int32), jax.random.randint(jax.random.fold_in(jax.random.fold_in(_rk, 1), 134), (16384,), 78, 99989, jnp.int32), jax.random.randint(jax.random.fold_in(jax.random.fold_in(_rk, 1), 135), (16384,), 0, 99989, jnp.int32), jax.random.randint(jax.random.fold_in(jax.random.fold_in(_rk, 1), 136), (16384,), 65, 100001, jnp.int32), jax.random.randint(jax.random.fold_in(jax.random.fold_in(_rk, 1), 137), (16384,), 36, 99976, jnp.int32), jax.random.randint(jax.random.fold_in(jax.random.fold_in(_rk, 1), 138), (16384,), 23, 99898, jnp.int32), jax.random.randint(jax.random.fold_in(jax.random.fold_in(_rk, 1), 139), (16384,), 3, 99981, jnp.int32), jax.random.randint(jax.random.fold_in(jax.random.fold_in(_rk, 1), 140), (16384,), 91, 99977, jnp.int32), jax.random.randint(jax.random.fold_in(jax.random.fold_in(_rk, 1), 141), (16384,), 29, 99995, jnp.int32), jax.random.randint(jax.random.fold_in(jax.random.fold_in(_rk, 1), 142), (16384,), 36, 99999, jnp.int32), jax.random.randint(jax.random.fold_in(jax.random.fold_in(_rk, 1), 143), (16384,), 21, 99981, jnp.int32), jax.random.randint(jax.random.fold_in(jax.random.fold_in(_rk, 1), 144), (16384,), 3, 99988, jnp.int32), jax.random.randint(jax.random.fold_in(jax.random.fold_in(_rk, 1), 145), (16384,), 79, 99981, jnp.int32), jax.random.randint(jax.random.fold_in(jax.random.fold_in(_rk, 1), 146), (16384,), 10, 100001, jnp.int32), jax.random.randint(jax.random.fold_in(jax.random.fold_in(_rk, 1), 147), (16384,), 78, 99972, jnp.int32), jax.random.randint(jax.random.fold_in(jax.random.fold_in(_rk, 1), 148), (16384,), 19, 99956, jnp.int32), jax.random.randint(jax.random.fold_in(jax.random.fold_in(_rk, 1), 149), (16384,), 47, 99970, jnp.int32), jax.random.randint(jax.random.fold_in(jax.random.fold_in(_rk, 1), 150), (16384,), 18, 99950, jnp.int32), jax.random.randint(jax.random.fold_in(jax.random.fold_in(_rk, 1), 151), (16384,), 5, 99986, jnp.int32), jax.random.randint(jax.random.fold_in(jax.random.fold_in(_rk, 1), 152), (16384,), 49, 99941, jnp.int32), jax.random.randint(jax.random.fold_in(jax.random.fold_in(_rk, 1), 153), (16384,), 59, 99947, jnp.int32), jax.random.randint(jax.random.fold_in(jax.random.fold_in(_rk, 1), 154), (16384,), 38, 99972, jnp.int32), jax.random.randint(jax.random.fold_in(jax.random.fold_in(_rk, 1), 155), (16384,), 38, 99962, jnp.int32), jax.random.randint(jax.random.fold_in(jax.random.fold_in(_rk, 1), 156), (16384,), 17, 99983, jnp.int32), jax.random.randint(jax.random.fold_in(jax.random.fold_in(_rk, 1), 157), (16384,), 34, 99961, jnp.int32), jax.random.randint(jax.random.fold_in(jax.random.fold_in(_rk, 1), 158), (16384,), 39, 99984, jnp.int32), jax.random.randint(jax.random.fold_in(jax.random.fold_in(_rk, 1), 159), (16384,), 2, 99997, jnp.int32), jax.random.randint(jax.random.fold_in(jax.random.fold_in(_rk, 1), 160), (16384,), 5, 99989, jnp.int32), jax.random.randint(jax.random.fold_in(jax.random.fold_in(_rk, 1), 161), (16384,), 10, 99969, jnp.int32), jax.random.randint(jax.random.fold_in(jax.random.fold_in(_rk, 1), 162), (16384,), 62, 99980, jnp.int32), jax.random.randint(jax.random.fold_in(jax.random.fold_in(_rk, 1), 163), (16384,), 52, 99980, jnp.int32), jax.random.randint(jax.random.fold_in(jax.random.fold_in(_rk, 1), 164), (16384,), 52, 99981, jnp.int32), jax.random.randint(jax.random.fold_in(jax.random.fold_in(_rk, 1), 165), (16384,), 7, 99993, jnp.int32), jax.random.randint(jax.random.fold_in(jax.random.fold_in(_rk, 1), 166), (16384,), 60, 99987, jnp.int32), jax.random.randint(jax.random.fold_in(jax.random.fold_in(_rk, 1), 167), (16384,), 14, 99998, jnp.int32), jax.random.randint(jax.random.fold_in(jax.random.fold_in(_rk, 1), 168), (16384,), 6, 99968, jnp.int32), jax.random.randint(jax.random.fold_in(jax.random.fold_in(_rk, 1), 169), (16384,), 4, 99981, jnp.int32), jax.random.randint(jax.random.fold_in(jax.random.fold_in(_rk, 1), 170), (16384,), 32, 99997, jnp.int32), jax.random.randint(jax.random.fold_in(jax.random.fold_in(_rk, 1), 171), (16384,), 0, 99977, jnp.int32), jax.random.randint(jax.random.fold_in(jax.random.fold_in(_rk, 1), 172), (16384,), 14, 99973, jnp.int32), jax.random.randint(jax.random.fold_in(jax.random.fold_in(_rk, 1), 173), (16384,), 7, 99971, jnp.int32), jax.random.randint(jax.random.fold_in(jax.random.fold_in(_rk, 1), 174), (16384,), 20, 99998, jnp.int32), jax.random.randint(jax.random.fold_in(jax.random.fold_in(_rk, 1), 175), (16384,), 11, 99998, jnp.int32), jax.random.randint(jax.random.fold_in(jax.random.fold_in(_rk, 1), 176), (16384,), 6, 99963, jnp.int32), jax.random.randint(jax.random.fold_in(jax.random.fold_in(_rk, 1), 177), (16384,), 20, 99994, jnp.int32), jax.random.randint(jax.random.fold_in(jax.random.fold_in(_rk, 1), 178), (16384,), 3, 99974, jnp.int32), jax.random.randint(jax.random.fold_in(jax.random.fold_in(_rk, 1), 179), (16384,), 36, 99961, jnp.int32), jax.random.randint(jax.random.fold_in(jax.random.fold_in(_rk, 1), 180), (16384,), 1, 99981, jnp.int32), jax.random.randint(jax.random.fold_in(jax.random.fold_in(_rk, 1), 181), (16384,), 9, 99999, jnp.int32), jax.random.randint(jax.random.fold_in(jax.random.fold_in(_rk, 1), 182), (16384,), 9, 99999, jnp.int32), jax.random.randint(jax.random.fold_in(jax.random.fold_in(_rk, 1), 183), (16384,), 21, 99999, jnp.int32), jax.random.randint(jax.random.fold_in(jax.random.fold_in(_rk, 1), 184), (16384,), 1, 99944, jnp.int32), jax.random.randint(jax.random.fold_in(jax.random.fold_in(_rk, 1), 185), (16384,), 54, 99999, jnp.int32), jax.random.randint(jax.random.fold_in(jax.random.fold_in(_rk, 1), 186), (16384,), 12, 99997, jnp.int32), jax.random.randint(jax.random.fold_in(jax.random.fold_in(_rk, 1), 187), (16384,), 49, 99982, jnp.int32), jax.random.randint(jax.random.fold_in(jax.random.fold_in(_rk, 1), 188), (16384,), 30, 99990, jnp.int32), jax.random.randint(jax.random.fold_in(jax.random.fold_in(_rk, 1), 189), (16384,), 19, 99994, jnp.int32), jax.random.randint(jax.random.fold_in(jax.random.fold_in(_rk, 1), 190), (16384,), 16, 99817, jnp.int32), jax.random.randint(jax.random.fold_in(jax.random.fold_in(_rk, 1), 191), (16384,), 8, 99900, jnp.int32), jax.random.randint(jax.random.fold_in(jax.random.fold_in(_rk, 1), 192), (16384,), 16, 100000, jnp.int32), jax.random.randint(jax.random.fold_in(jax.random.fold_in(_rk, 1), 193), (16384,), 3, 99958, jnp.int32), jax.random.randint(jax.random.fold_in(jax.random.fold_in(_rk, 1), 194), (16384,), 25, 99994, jnp.int32), jax.random.randint(jax.random.fold_in(jax.random.fold_in(_rk, 1), 195), (16384,), 22, 99942, jnp.int32), jax.random.randint(jax.random.fold_in(jax.random.fold_in(_rk, 1), 196), (16384,), 0, 99998, jnp.int32), jax.random.randint(jax.random.fold_in(jax.random.fold_in(_rk, 1), 197), (16384,), 24, 99970, jnp.int32), jax.random.randint(jax.random.fold_in(jax.random.fold_in(_rk, 1), 198), (16384,), 31, 99991, jnp.int32), jax.random.randint(jax.random.fold_in(jax.random.fold_in(_rk, 1), 199), (16384,), 69, 99983, jnp.int32), jax.random.randint(jax.random.fold_in(jax.random.fold_in(_rk, 1), 200), (16384,), 25, 99980, jnp.int32)], axis=1)
        return r_x
    r_x = _rec_inputs()
    def _L0_rec_setup():
        import jax, jax.numpy as jnp
        import numpy as np
        EPS = 1e-09

        def dice(x, alpha):
            norm = (x - x.mean(axis=0)) / jnp.sqrt(x.var(axis=0, ddof=1) + EPS)
            p = jax.nn.sigmoid(norm)
            return alpha * x * (1.0 - p) + x * p
        key = jax.random.key(seed)
        ks = jax.random.split(key, 12)
        B, S, D = (4096, 200, 64)
        V = 100000 + 1
        x = jax.random.randint(ks[0], (B, S + 1), 0, V, dtype=jnp.int64)

        def lin(k, fan_in, fan_out):
            bound = 1.0 / np.sqrt(fan_in)
            kw, kb = jax.random.split(k)
            W = jax.random.uniform(kw, (fan_in, fan_out), jnp.float32, -bound, bound)
            b = jax.random.uniform(kb, (fan_out,), jnp.float32, -bound, bound)
            return (W, b)
        emb = jax.random.normal(ks[1], (V, D), jnp.float32)
        au_W1, au_b1 = lin(ks[2], 4 * D, 32)
        au_W2, au_b2 = lin(ks[3], 32, 16)
        au_W3, au_b3 = lin(ks[4], 16, 1)
        au_a1 = jnp.zeros((1,), jnp.float32)
        au_a2 = jnp.zeros((1,), jnp.float32)
        mlp_W1, mlp_b1 = lin(ks[5], 2 * D, 64)
        mlp_W2, mlp_b2 = lin(ks[6], 64, 32)
        mlp_W3, mlp_b3 = lin(ks[7], 32, 1)
        return {'x': x, 'emb': emb, 'au_W1': au_W1, 'au_b1': au_b1, 'au_a1': au_a1, 'au_W2': au_W2, 'au_b2': au_b2, 'au_a2': au_a2, 'au_W3': au_W3, 'au_b3': au_b3, 'mlp_W1': mlp_W1, 'mlp_b1': mlp_b1, 'mlp_W2': mlp_W2, 'mlp_b2': mlp_b2, 'mlp_W3': mlp_W3, 'mlp_b3': mlp_b3}
    _L0_rec_all = _L0_rec_setup()
    _L0_rec_in = {k: v for k, v in _L0_rec_all.items() if k in ('emb', 'au_W1', 'au_b1', 'au_a1', 'au_W2', 'au_b2', 'au_a2', 'au_W3', 'au_b3', 'mlp_W1', 'mlp_b1', 'mlp_W2', 'mlp_b2', 'mlp_W3', 'mlp_b3', )}
    del _L0_rec_all

    return {
        "r_x": r_x,
        "L0_rec_emb": _L0_rec_in["emb"],
        "L0_rec_au_W1": _L0_rec_in["au_W1"],
        "L0_rec_au_b1": _L0_rec_in["au_b1"],
        "L0_rec_au_a1": _L0_rec_in["au_a1"],
        "L0_rec_au_W2": _L0_rec_in["au_W2"],
        "L0_rec_au_b2": _L0_rec_in["au_b2"],
        "L0_rec_au_a2": _L0_rec_in["au_a2"],
        "L0_rec_au_W3": _L0_rec_in["au_W3"],
        "L0_rec_au_b3": _L0_rec_in["au_b3"],
        "L0_rec_mlp_W1": _L0_rec_in["mlp_W1"],
        "L0_rec_mlp_b1": _L0_rec_in["mlp_b1"],
        "L0_rec_mlp_W2": _L0_rec_in["mlp_W2"],
        "L0_rec_mlp_b2": _L0_rec_in["mlp_b2"],
        "L0_rec_mlp_W3": _L0_rec_in["mlp_W3"],
        "L0_rec_mlp_b3": _L0_rec_in["mlp_b3"],
    }

def reference(r_x, L0_rec_emb, L0_rec_au_W1, L0_rec_au_b1, L0_rec_au_a1, L0_rec_au_W2, L0_rec_au_b2, L0_rec_au_a2, L0_rec_au_W3, L0_rec_au_b3, L0_rec_mlp_W1, L0_rec_mlp_b1, L0_rec_mlp_W2, L0_rec_mlp_b2, L0_rec_mlp_W3, L0_rec_mlp_b3):
    import jax
    import jax.numpy as jnp
    def _L0_rec_ref(x, emb, au_W1, au_b1, au_a1, au_W2, au_b2, au_a2, au_W3, au_b3, mlp_W1, mlp_b1, mlp_W2, mlp_b2, mlp_W3, mlp_b3):
        import jax, jax.numpy as jnp
        import numpy as np
        EPS = 1e-09

        def dice(x, alpha):
            norm = (x - x.mean(axis=0)) / jnp.sqrt(x.var(axis=0, ddof=1) + EPS)
            p = jax.nn.sigmoid(norm)
            return alpha * x * (1.0 - p) + x * p
        behaviors = x[:, :-1]
        mask = (behaviors > 0).astype(jnp.float32)[..., None]
        query = emb[x[:, -1]]
        ub = emb[behaviors] * mask
        q = jnp.broadcast_to(query[:, None, :], ub.shape)
        feat = jnp.concatenate([q, ub, q - ub, q * ub], axis=-1)
        h = dice(feat @ au_W1 + au_b1, au_a1)
        h = dice(h @ au_W2 + au_b2, au_a2)
        score = h @ au_W3 + au_b3
        interest = (ub * score * mask).sum(axis=1)
        comb = jnp.concatenate([interest, query], axis=-1)
        m = jax.nn.relu(comb @ mlp_W1 + mlp_b1)
        m = jax.nn.relu(m @ mlp_W2 + mlp_b2)
        out = jax.nn.sigmoid((m @ mlp_W3 + mlp_b3)[:, 0])
        return out

    y = _L0_rec_ref(r_x, L0_rec_emb, L0_rec_au_W1, L0_rec_au_b1, L0_rec_au_a1, L0_rec_au_W2, L0_rec_au_b2, L0_rec_au_a2, L0_rec_au_W3, L0_rec_au_b3, L0_rec_mlp_W1, L0_rec_mlp_b1, L0_rec_mlp_W2, L0_rec_mlp_b2, L0_rec_mlp_W3, L0_rec_mlp_b3)
    return y


_drawn_inputs = setup_inputs


def setup_inputs(seed=0):
    import zlib

    import numpy as np

    out = dict(_drawn_inputs(seed))
    spreads = {}
    factors = {'L0_rec_au_b1': 23.542,
     'L0_rec_au_b2': 4.523,
     'L0_rec_mlp_b1': 7.843,
     'L0_rec_mlp_b2': 4.17}
    for name, (base, spread) in spreads.items():
        noise = np.random.default_rng([zlib.crc32(name.encode()), seed]).standard_normal(out[name].shape)
        drawn = base * np.exp(spread * noise) if base else spread * noise
        out[name] = jnp.asarray(drawn.astype(out[name].dtype))
    for name, factor in factors.items():
        out[name] = (out[name] * factor).astype(out[name].dtype)
    return out
```

```python
from contextlib import ExitStack

import numpy as np

import concourse.bass as bass
from concourse import mybir

F32 = mybir.dt.float32
I32 = mybir.dt.int32
ALU = mybir.AluOpType
ACT = mybir.ActivationFunctionType

P = 128
EPS = 1e-9
COLS = 512
CHUNK_TILES = 8
SP_GROUP = 16
LOOKAHEAD = 2


def din_kernel(nc, ids, emb, au_W1, au_b1, au_a1, au_W2, au_b2, au_a2, au_W3, au_b3,
               mlp_W1, mlp_b1, mlp_W2, mlp_b2, mlp_W3, mlp_b3, identity, same32, same16, out):
    V, D = emb.shape
    B = out.shape[0] * out.shape[1]
    S = ids.shape[0] - 1 - LOOKAHEAD
    TILES = B // P
    H1 = au_W1.shape[1]
    H2 = au_W2.shape[1]
    M1 = mlp_W1.shape[1]
    M2 = mlp_W2.shape[1]
    CHUNKS = TILES // CHUNK_TILES
    PAIRS = CHUNK_TILES // 2
    K1 = CHUNKS // 2
    K2 = K1 // 2
    N1 = K1 * COLS
    N2 = K2 * COLS
    WIDE = 2 * COLS
    RING = 3
    SP_TILE = TILES - 1
    UNBIAS = float(B) / float(B - 1)
    assert 2 * D == P and 4 * H1 == P and 8 * H2 == P and S % 2 == 0

    with ExitStack() as ctx:
        def sb(name, shape, dt=F32):
            return ctx.enter_context(nc.sbuf_tensor(name, shape, dt))

        def ps(name, shape):
            return ctx.enter_context(nc.psum_tensor(name, shape, F32))

        def sem(name):
            return ctx.enter_context(nc.semaphore(name))

        masked_emb = nc.dram_tensor("masked_emb", (V, D), F32, kind="Internal").ap()

        rows = sb("rows", [P, 2, TILES, D])
        queryT = sb("queryT", [P, CHUNKS * COLS])
        query_part = sb("query_part", [P, N1])
        interest = sb("interest", [P, TILES, D])
        hidden = sb("hidden", [P, N1])
        gate1 = sb("gate1", [P, N1])
        z1 = hidden
        z2 = hidden[:, 0:N2]
        gate2 = hidden[:, N2:2 * N2]
        featT = sb("featT", [P, RING, COLS])
        prodT = sb("prodT", [P, RING, COLS])
        ids_raw = sb("ids_raw", [P, 2, TILES], I32)
        ids_ok = sb("ids_ok", [P, 2, TILES], I32)
        sp_ids = sb("sp_ids", [1, 2, P], I32)
        query_ids = sb("query_ids", [P, 2, TILES], I32)
        ident = sb("ident", [P, P])
        same1 = sb("same1", [P, P])
        same2 = sb("same2", [P, P])
        wparts = sb("wparts", [P, 4, 2 * H1])
        w_query = sb("w_query", [P, 2 * H1])
        w_row = sb("w_row", [P, 2 * H1])
        w_prod = wparts[:, 3, :]
        w2 = sb("w2", [P, 4 * H2])
        w3 = sb("w3", [P, 8])
        b1 = sb("b1", [P, 1])
        b2 = sb("b2", [P, 1])
        b3 = sb("b3", [P, 1])
        alphas = sb("alphas", [P, 2])
        one_minus = sb("one_minus", [P, 2])
        eps = sb("eps", [P, 1])
        zero_row = sb("zero_row", [1, D])
        stats1 = sb("stats1", [P, K1, 6])
        stats2 = sb("stats2", [P, K2, 6])
        moments = sb("moments", [P, 2, 2])
        offset = sb("offset", [P, 2])
        spread = sb("spread", [P, 2])
        std = sb("std", [P, 2])
        rstd = sb("rstd", [P, 2])
        shift = sb("shift", [P, 2])
        m_w1i = sb("m_w1i", [P, 2 * M1])
        m_w1q = sb("m_w1q", [P, 2 * M1])
        m_w2 = sb("m_w2", [P, 2 * M2])
        m_w3 = sb("m_w3", [2 * M2, 2])
        m_b1 = sb("m_b1", [P, 1])
        m_b2 = sb("m_b2", [2 * M2, 1])
        m_b3 = sb("m_b3", [P, 1])
        result = sb("result", [P, TILES])

        def mlp_h2(c):
            return (hidden if c < K1 else gate1)[0:2 * M2, (c % K1) * COLS:(c % K1 + 1) * COLS]

        turned = ps("turned", [P, 2, COLS])
        z1_ps = ps("z1_ps", [P, 2, COLS])
        z2_ps = ps("z2_ps", [P, 2, COLS])
        stat_ps = ps("stat_ps", [P, COLS])
        score_ps = ps("score_ps", [P, COLS])
        mean_ps = [stat_ps[:, 0:1], stat_ps[:, 2:3]]
        var_ps = [stat_ps[:, 1:2], stat_ps[:, 3:4]]

        consts_loaded = sem("consts_loaded")
        cleared = sem("cleared")
        zero_ready = sem("zero_ready")
        table_ready = sem("table_ready")
        weights_ready = sem("weights_ready")
        query_ids_loaded = sem("query_ids_loaded")
        query_ids_ready = sem("query_ids_ready")
        query_rows = sem("query_rows")
        query_turned = sem("query_turned")
        queryT_ready = sem("queryT_ready")
        query_projected = sem("query_projected")
        query_part_ready = sem("query_part_ready")
        z2_stats_seen = sem("z2_stats_seen")
        ids_loaded = [sem(f"ids_loaded{p}") for p in range(2)]
        ids_ready = sem("ids_ready")
        rows_free = sem("rows_free")
        gather_begun = sem("gather_begun")
        gathered = [[sem(f"gathered{p}_{c}") for c in range(CHUNKS)] for p in range(2)]
        sp_ids_ready = [sem(f"sp_ids_ready{p}") for p in range(2)]
        sp_begun = sem("sp_begun")
        sp_gathered = [[sem(f"sp_gathered{p}_{g}") for g in range(P // SP_GROUP)] for p in range(2)]
        chunk_turned = sem("chunk_turned")
        chunk_copied = sem("chunk_copied")
        chunk_times_query = sem("chunk_times_query")
        chunk_projected = sem("chunk_projected")
        z1_ready = sem("z1_ready")
        z1_stats = sem("z1_stats")
        moments_ready = [sem(f"moments_ready{n}") for n in (1, 2)]
        mean_ready = [sem(f"mean_ready{n}") for n in (1, 2)]
        offset_ready = [sem(f"offset_ready{n}") for n in (1, 2)]
        spread_ready = [sem(f"spread_ready{n}") for n in (1, 2)]
        var_ready = [sem(f"var_ready{n}") for n in (1, 2)]
        std_ready = [sem(f"std_ready{n}") for n in (1, 2)]
        rstd_ready = [sem(f"rstd_ready{n}") for n in (1, 2)]
        shift_ready = [sem(f"shift_ready{n}") for n in (1, 2)]
        sigmoid_done = [sem(f"sigmoid_done{n}") for n in (1, 2)]
        gate_ready = [sem(f"gate_ready{n}") for n in (1, 2)]
        h_ready = [sem(f"h_ready{n}") for n in (1, 2)]
        z2_projected = sem("z2_projected")
        z2_ready = sem("z2_ready")
        z2_stats = sem("z2_stats")
        scores_in_psum = sem("scores_in_psum")
        score_ready = sem("score_ready")
        weighted = sem("weighted")
        interest_cleared = sem("interest_cleared")
        interest_done = sem("interest_done")
        int_turned = sem("int_turned")
        int_copied = sem("int_copied")
        mlp1_done = sem("mlp1_done")
        mlp1_relu = sem("mlp1_relu")
        mlp2_done = sem("mlp2_done")
        mlp2_relu = sem("mlp2_relu")
        logits_done = sem("logits_done")
        result_ready = sem("result_ready")
        stored = sem("stored")

        block = ctx.enter_context(nc.Block())

        def column(v):
            return v.rearrange("(p a) -> p a", a=1)

        n_consts = 0

        @block.sync
        def _(sp):
            nonlocal n_consts

            def const(dst, src):
                nonlocal n_consts
                sp.dma_start(dst, src).then_inc(consts_loaded, 16)
                n_consts += 1

            sp.dma_start(query_ids[:, 0, :], ids[S]).then_inc(query_ids_loaded, 16)
            for s in range(2):
                sp.dma_start(ids_raw[:, s, :], ids[s]).then_inc(ids_loaded[s], 16)
            const(ident[:, :], identity)
            const(same1[:, :], same32)
            const(same2[:, :], same16)
            with nc.allow_non_contiguous_dma(reason="biases, one value in a partition"):
                for n in range(4):
                    const(b1[n * H1:(n + 1) * H1, :], column(au_b1))
                for n in range(8):
                    const(b2[n * H2:(n + 1) * H2, :], column(au_b2))
                const(b3[:, :], column(au_b3).to_broadcast([P, 1]))
                const(alphas[:, 0:1], column(au_a1).to_broadcast([P, 1]))
                const(alphas[:, 1:2], column(au_a2).to_broadcast([P, 1]))
                for par in range(2):
                    const(m_b1[par * M1:(par + 1) * M1, :], column(mlp_b1))
                    const(m_b2[par * M2:(par + 1) * M2, :], column(mlp_b2))
                const(m_b3[:, :], column(mlp_b3).to_broadcast([P, 1]))
                sp.wait_ge(cleared, 1)
                for par in range(2):
                    q = slice(par * D, (par + 1) * D)
                    const(wparts[q, :, par * H1:(par + 1) * H1], au_W1.rearrange("(k d) c -> d k c", d=D))
                    const(m_w1i[q, par * M1:(par + 1) * M1], mlp_W1[0:D, :])
                    const(m_w1q[q, par * M1:(par + 1) * M1], mlp_W1[D:2 * D, :])
                    const(m_w2[par * M1:(par + 1) * M1, par * M2:(par + 1) * M2], mlp_W2)
                    const(m_w3[par * M2:(par + 1) * M2, par:par + 1], mlp_W3)
                for n in range(4):
                    const(w2[n * H1:(n + 1) * H1, n * H2:(n + 1) * H2], au_W2)
                for n in range(8):
                    const(w3[n * H2:(n + 1) * H2, n:n + 1], au_W3)
            sp.wait_ge(table_ready, 32)
            with sp.Fori(0, S // 2) as i:
                for par in range(2):
                    s = 2 * i + par
                    sp.wait_ge(ids_ready, s + 1)
                    sp.dma_start(ids_raw[:, par, :], ids[s + LOOKAHEAD]).then_inc(ids_loaded[par], 16)
                    with nc.allow_non_contiguous_dma(reason="one id in a partition"):
                        sp.dma_start(sp_ids[:, par, :], ids_ok[:, par, SP_TILE:SP_TILE + 1]
                                     ).then_inc(sp_ids_ready[par], 16)
                    sp.wait_ge(rows_free, s + 1)
                    sp.wait_ge(sp_ids_ready[par], 16 * i + 16)
                    sp.sem_inc(sp_begun, 1)
                    for g in range(P // SP_GROUP):
                        _, row_ids = nc.values_load_multi_w_load_instructions(
                            sp_ids[0:1, par, g * SP_GROUP:(g + 1) * SP_GROUP],
                            engines=[mybir.EngineType.SP], min_val=0, max_val=V - 1)
                        for n, row_id in enumerate(row_ids):
                            lane = g * SP_GROUP + n
                            sp.dma_start(rows[lane:lane + 1, par, SP_TILE, :],
                                         masked_emb[bass.ds(row_id, 1), :]).then_inc(sp_gathered[par][g], 16)
            sp.wait_ge(result_ready, 1)
            sp.dma_start(out, result[:, :]).then_inc(stored, 16)
            sp.wait_ge(stored, 16)
            for par in range(2):
                sp.wait_ge(ids_loaded[par], 16 * (S // 2 + 1))

        @block.gpsimd
        def _(pool):
            pool.wait_ge(query_ids_ready, 1)
            for t in range(TILES):
                pool.indirect_dma_start(interest[:, t, :], None, emb,
                                        bass.IndirectOffsetOnAxis(query_ids[:, 1, t:t + 1], 0)
                                        ).then_inc(query_rows, 16)
            pool.wait_ge(table_ready, 32)
            with nc.Fori(0, S // 2, engines=[mybir.EngineType.Pool], hint_back_edge=True) as i:
                for par in range(2):
                    pool.wait_ge(rows_free, 2 * i + par + 1)
                    pool.wait_ge(ids_ready, 2 * i + par + 1)
                    pool.sem_inc(gather_begun, 1)
                    for t in range(SP_TILE):
                        pool.indirect_dma_start(rows[:, par, t, :], None, masked_emb,
                                                bass.IndirectOffsetOnAxis(ids_ok[:, par, t:t + 1], 0)
                                                ).then_inc(gathered[par][t // CHUNK_TILES], 16)

        @block.tensor
        def _(pe):
            pe.wait_ge(consts_loaded, 16 * n_consts)
            pe.wait_ge(query_rows, 16 * TILES)

            def turn(src, c):
                for r in range(PAIRS):
                    last = pe.transpose(turned[:, c % 2, r * P:(r + 1) * P],
                                        src[:, 2 * r:2 * r + 2, :].rearrange("p t d -> p (t d)"), ident[:, :])
                return last

            def chunk_rows(x, c):
                return x[:, CHUNK_TILES * c:CHUNK_TILES * (c + 1), :]

            def query_projection(c):
                pe.wait_ge(queryT_ready, c + 1)
                if c == 0:
                    pe.wait_ge(weights_ready, 2)
                if c % 2 == 0 and c >= 4:
                    pe.wait_ge(query_part_ready, c // 2 - 1)
                g = c % 2
                mm = pe.matmul(z1_ps[g * D:(g + 1) * D, (c // 2) % 2, :], w_query[:, :],
                               queryT[:, c * COLS:(c + 1) * COLS], start=True, stop=True)
                if g:
                    mm.then_inc(query_projected, 1)

            for c in range(CHUNKS):
                if c >= 2:
                    pe.wait_ge(queryT_ready, c - 1)
                turn(chunk_rows(interest, c), c).then_inc(query_turned, 1)
                if c >= 1:
                    query_projection(c - 1)
            query_projection(CHUNKS - 1)
            pe.wait_ge(query_part_ready, K1)

            def step(i, par):
                s = 2 * i + par

                def projection(c):
                    pe.wait_ge(chunk_copied, s * CHUNKS + c + 1)
                    g = c % 2
                    if g == 0 and c >= 4:
                        pe.wait_ge(z1_ready, s * K1 + c // 2 - 1)
                    z = z1_ps[g * D:(g + 1) * D, (c // 2) % 2, :]
                    pe.matmul(z, w_row[:, :], featT[:, c % RING, :], start=True, stop=False)
                    pe.wait_ge(chunk_times_query, s * CHUNKS + c + 1)
                    pe.matmul(z, w_prod, prodT[:, c % RING, :], start=False, stop=True
                              ).then_inc(chunk_projected, 1)

                for c in range(CHUNKS):
                    if c < CHUNKS - 1:
                        pe.wait_ge(gathered[par][c], (i + 1) * (16 * CHUNK_TILES))
                    else:
                        pe.wait_ge(gathered[par][c], (i + 1) * (16 * (CHUNK_TILES - 1)))
                        for q in sp_gathered[par]:
                            pe.wait_ge(q, (i + 1) * (16 * SP_GROUP))
                    if c >= 2:
                        pe.wait_ge(chunk_times_query, s * CHUNKS + c - 1)
                    turn(chunk_rows(rows[:, par, :, :], c), c).then_inc(chunk_turned, 1)
                    if c >= 1:
                        projection(c - 1)
                projection(CHUNKS - 1)

                def batch_statistics(n, same):
                    pe.wait_ge(moments_ready[n], s + 1)
                    pe.matmul(mean_ps[n], same, moments[:, n, 0:1], start=True, stop=True
                              ).then_inc(mean_ready[n], 1)
                    pe.wait_ge(spread_ready[n], s + 1)
                    pe.matmul(var_ps[n], same, spread[:, n:n + 1], start=True, stop=True
                              ).then_inc(var_ready[n], 1)

                batch_statistics(0, same1[:, :])
                for k in range(K1):
                    if k % 2 == 0 and k >= 4:
                        pe.wait_ge(z2_ready, s * K2 + k // 2 - 1)
                    pe.wait_ge(h_ready[0], s * K1 + k + 1)
                    half = k % 2
                    mm = pe.matmul(z2_ps[half * D:(half + 1) * D, (k // 2) % 2, :], w2[:, :],
                                   gate1[:, k * COLS:(k + 1) * COLS], start=True, stop=True)
                    if half:
                        mm.then_inc(z2_projected, 1)
                batch_statistics(1, same2[:, :])
                for n in range(N2 // P):
                    if n % PAIRS == 0:
                        pe.wait_ge(h_ready[1], s * K2 + n // PAIRS + 1)
                    j, r = n // PAIRS, n % PAIRS
                    dst = score_ps[:, 32 * j:32 * j + 32].rearrange("p (h r a) -> p r h a", r=PAIRS, a=2)[:, r]
                    mm = pe.matmul(dst, gate2[:, n * P:(n + 1) * P], w3[:, :], start=True, stop=True)
                mm.then_inc(scores_in_psum, 1)

            with pe.Fori(0, S // 2) as i:
                for par in range(2):
                    step(i, par)

            def mlp1(c):
                if c >= 2:
                    pe.wait_ge(mlp1_relu, c - 1)
                z = z1_ps[:, c % 2, :]
                pe.matmul(z, m_w1q[:, :], queryT[:, c * COLS:(c + 1) * COLS], start=True, stop=False)
                pe.wait_ge(int_copied, c + 1)
                pe.matmul(z, m_w1i[:, :], featT[:, c % RING, :], start=False, stop=True).then_inc(mlp1_done, 1)

            def mlp2(c):
                if c >= 1:
                    pe.wait_ge(mlp2_relu, c)
                pe.wait_ge(mlp1_relu, c + 1)
                pe.matmul(stat_ps[0:2 * M2, :], m_w2[:, :], prodT[:, c % RING, :],
                          start=True, stop=True).then_inc(mlp2_done, 1)

            def logits(c):
                pe.wait_ge(mlp2_relu, c + 1)
                for r in range(PAIRS):
                    t = CHUNK_TILES * c + 2 * r
                    last = pe.matmul(score_ps[:, t:t + 2], mlp_h2(c)[:, r * P:(r + 1) * P], m_w3[:, :],
                                     start=True, stop=True)
                return last

            for c in range(CHUNKS + 2):
                if c < CHUNKS:
                    if c >= 2:
                        pe.wait_ge(int_copied, c - 1)
                    pe.wait_ge(interest_done, (S - 1) * CHUNKS + c + 1)
                    turn(chunk_rows(interest, c), c).then_inc(int_turned, 1)
                if 0 <= c - 1 < CHUNKS:
                    mlp1(c - 1)
                if c >= 2:
                    mlp2(c - 2)
                if c == CHUNKS:
                    pe.wait_ge(weighted, S * CHUNKS)
                if c >= CHUNKS:
                    for n in range((c - CHUNKS) * (CHUNKS - 2), min((c - CHUNKS + 1) * (CHUNKS - 2), CHUNKS)):
                        mm = logits(n)
            mm.then_inc(logits_done, 1)

        @block.scalar
        def _(act):
            act.dma_start(masked_emb[1:V, :].rearrange("(a b) d -> a (b d)", a=32),
                          emb[1:V, :].rearrange("(a b) d -> a (b d)", a=32)).then_inc(table_ready, 16)
            act.wait_ge(zero_ready, 1)
            act.dma_start(masked_emb[0:1, :], zero_row[:, :]).then_inc(table_ready, 16)
            for c in range(CHUNKS):
                act.wait_ge(query_turned, c + 1)
                act.activation(queryT[:, c * COLS:(c + 1) * COLS], turned[:, c % 2, :], ACT.Copy
                               ).then_inc(queryT_ready, 1)

            def step(i, par):
                s = 2 * i + par
                for c in range(CHUNKS):
                    act.wait_ge(chunk_turned, s * CHUNKS + c + 1)
                    if c >= RING:
                        act.wait_ge(chunk_projected, s * CHUNKS + c - RING + 1)
                    act.activation(featT[:, c % RING, :], turned[:, c % 2, :], ACT.Copy
                                   ).then_inc(chunk_copied, 1)

                def gates(n, z, gate, width):
                    count = width // WIDE
                    act.wait_ge(var_ready[n], s + 1)
                    act.activation(std[:, n:n + 1], var_ps[n], ACT.Sqrt, bias=eps[:, :], scale=UNBIAS
                                   ).then_inc(std_ready[n], 1)
                    act.wait_ge(shift_ready[n], s + 1)
                    def sigmoid(w):
                        q = slice(w * WIDE, (w + 1) * WIDE)
                        act.activation(gate[:, q], z[:, q], ACT.Sigmoid, bias=shift[:, n:n + 1],
                                       scale=rstd[:, n:n + 1]).then_inc(sigmoid_done[n], 1)

                    sigmoid(0)
                    for k in range(width // COLS):
                        q = slice(k * COLS, (k + 1) * COLS)
                        if k % (WIDE // COLS) == 0:
                            w = k // (WIDE // COLS)
                            if w + 1 < count:
                                sigmoid(w + 1)
                            act.wait_ge(sigmoid_done[n], s * count + w + 1)
                        if k >= 2:
                            act.wait_ge(h_ready[n], s * (width // COLS) + k - 1)
                        act.activation(turned[:, k % 2, :], gate[:, q], ACT.Identity, bias=alphas[:, n:n + 1],
                                       scale=one_minus[:, n:n + 1]).then_inc(gate_ready[n], 1)

                gates(0, z1, gate1, N1)
                for j in range(K2):
                    act.wait_ge(z2_projected, s * K2 + j + 1)
                    act.activation(z2[:, j * COLS:(j + 1) * COLS], z2_ps[:, j % 2, :], ACT.Identity,
                                   bias=b2[:, :]).then_inc(z2_ready, 1)
                gates(1, z2, gate2, N2)
                act.wait_ge(scores_in_psum, s + 1)
                act.activation(score_ps[:, 0:TILES], score_ps[:, 0:TILES], ACT.Identity, bias=b3[:, :]
                               ).then_inc(score_ready, 1)

            with act.Fori(0, S // 2) as i:
                for par in range(2):
                    step(i, par)

            for c in range(CHUNKS + 2):
                if c < CHUNKS:
                    act.wait_ge(int_turned, c + 1)
                    if c >= RING:
                        act.wait_ge(mlp1_done, c - RING + 1)
                    act.activation(featT[:, c % RING, :], turned[:, c % 2, :], ACT.Copy
                                   ).then_inc(int_copied, 1)
                if c >= 2:
                    act.wait_ge(mlp2_done, c - 1)
                    act.activation(mlp_h2(c - 2), stat_ps[0:2 * M2, :], ACT.Relu, bias=m_b2[:, :]
                                   ).then_inc(mlp2_relu, 1)
                if 0 <= c - 1 < CHUNKS:
                    act.wait_ge(mlp1_done, c)
                    if c - 1 >= RING:
                        act.wait_ge(mlp2_done, c - RING)
                    act.activation(prodT[:, (c - 1) % RING, :], z1_ps[:, (c - 1) % 2, :], ACT.Relu,
                                   bias=m_b1[:, :]).then_inc(mlp1_relu, 1)
            act.wait_ge(logits_done, 1)
            act.activation(result[:, :], score_ps[:, 0:TILES], ACT.Sigmoid, bias=m_b3[:, :]
                           ).then_inc(result_ready, 1)

        @block.vector
        def _(dve):
            def clamp(dst, src):
                return dve.tensor_scalar(dst, src, 0, V - 1, ALU.max, ALU.min)

            dve.wait_ge(query_ids_loaded, 16)
            clamp(query_ids[:, 1, :], query_ids[:, 0, :]).then_inc(query_ids_ready, 1)
            dve.memset(zero_row[:, :], 0.0).then_inc(zero_ready, 1)
            dve.sem_inc(rows_free, 2)
            for w in (wparts, m_w1i, m_w1q, m_w2, m_w3, w2, w3):
                m = dve.memset(w[:], 0.0)
            m.then_inc(cleared, 1)
            dve.memset(eps[:, :], EPS)
            for s in range(2):
                dve.wait_ge(ids_loaded[s], 16)
                clamp(ids_ok[:, s, :], ids_raw[:, s, :]).then_inc(ids_ready, 1)
            dve.wait_ge(consts_loaded, 16 * n_consts)
            dve.tensor_tensor(w_query[:, :], wparts[:, 0, :], wparts[:, 2, :], ALU.add).then_inc(weights_ready, 1)
            dve.tensor_tensor(w_row[:, :], wparts[:, 1, :], wparts[:, 2, :], ALU.subtract).then_inc(weights_ready, 1)
            dve.tensor_scalar(one_minus[:, :], alphas[:, :], -1.0, 1.0, ALU.mult, ALU.add).then_inc(weights_ready, 1)
            for k in range(K1):
                dve.wait_ge(query_projected, k + 1)
                dve.tensor_scalar(query_part[:, k * COLS:(k + 1) * COLS], z1_ps[:, k % 2, :], b1[:, :], None,
                                  ALU.add).then_inc(query_part_ready, 1)
            dve.memset(interest[:], 0.0).then_inc(interest_cleared, 1)

            def step(i, par):
                s = 2 * i + par

                def bank(k):
                    q = slice(k * COLS, (k + 1) * COLS)
                    dve.wait_ge(chunk_projected, s * CHUNKS + 2 * k + 2)
                    if k == 0:
                        dve.wait_ge(query_part_ready, K1)
                    dve.tensor_tensor(z1[:, q], z1_ps[:, k % 2, :], query_part[:, q], ALU.add
                                      ).then_inc(z1_ready, 1)
                    if k >= 1:
                        bank_statistics(k - 1)

                def bank_statistics(k):
                    dve.wait_ge(z1_ready, s * K1 + k + 1)
                    dve.bn_stats(stats1[:, k, :], z1[:, k * COLS:(k + 1) * COLS]).then_inc(z1_stats, 1)

                for c in range(CHUNKS):
                    dve.wait_ge(chunk_copied, s * CHUNKS + c + 1)
                    if c >= RING:
                        dve.wait_ge(chunk_projected, s * CHUNKS + c - RING + 1)
                    dve.tensor_tensor(prodT[:, c % RING, :], turned[:, c % 2, :],
                                      queryT[:, c * COLS:(c + 1) * COLS], ALU.mult
                                      ).then_inc(chunk_times_query, 1)
                    if c >= 3 and c % 2 == 1:
                        bank((c - 3) // 2)
                bank(K1 - 1)
                bank_statistics(K1 - 1)

                def statistics(n, stats):
                    dve.bn_aggr(moments[:, n, :], stats[:].rearrange("p k x -> p (k x)")
                                ).then_inc(moments_ready[n], 1)
                    dve.wait_ge(mean_ready[n], s + 1)
                    dve.tensor_tensor(offset[:, n:n + 1], moments[:, n, 0:1], mean_ps[n], ALU.subtract
                                      ).then_inc(offset_ready[n], 1)
                    dve.wait_ge(offset_ready[n], s + 1)
                    dve.scalar_tensor_tensor(spread[:, n:n + 1], offset[:, n:n + 1], offset[:, n:n + 1],
                                             moments[:, n, 1:2], ALU.mult, ALU.add).then_inc(spread_ready[n], 1)
                    dve.wait_ge(std_ready[n], s + 1)
                    dve.reciprocal(rstd[:, n:n + 1], std[:, n:n + 1]).then_inc(rstd_ready[n], 1)
                    dve.wait_ge(rstd_ready[n], s + 1)
                    dve.scalar_tensor_tensor(shift[:, n:n + 1], mean_ps[n], -1.0, rstd[:, n:n + 1],
                                             ALU.mult, ALU.mult).then_inc(shift_ready[n], 1)

                def gated(n, z, gate, width):
                    for k in range(width // COLS):
                        q = slice(k * COLS, (k + 1) * COLS)
                        dve.wait_ge(gate_ready[n], s * (width // COLS) + k + 1)
                        dve.tensor_tensor(gate[:, q], turned[:, k % 2, :], z[:, q], ALU.mult
                                          ).then_inc(h_ready[n], 1)

                dve.wait_ge(ids_loaded[par], (i + 2) * 16)
                dve.wait_ge(z1_stats, s * K1 + K1)
                clamp(ids_ok[:, par, :], ids_raw[:, par, :]).then_inc(ids_ready, 1)
                statistics(0, stats1)
                gated(0, z1, gate1, N1)
                for j in range(K2):
                    dve.wait_ge(z2_ready, s * K2 + j + 1)
                    dve.bn_stats(stats2[:, j, :], z2[:, j * COLS:(j + 1) * COLS]).then_inc(z2_stats, 1)
                dve.wait_ge(z2_stats, s * K2 + K2)
                dve.sem_inc(z2_stats_seen, 1)
                statistics(1, stats2)
                gated(1, z2, gate2, N2)
                def add_chunk(c):
                    t = slice(c * CHUNK_TILES, (c + 1) * CHUNK_TILES)
                    if c == 0:
                        dve.wait_ge(interest_cleared, 1)
                    dve.wait_ge(weighted, s * CHUNKS + c + 1)
                    dve.tensor_tensor(interest[:, t, :], interest[:, t, :],
                                      z2_ps[:, c % 2, :].rearrange("p (t d) -> p t d", d=D), ALU.add
                                      ).then_inc(interest_done, 1)

                dve.wait_ge(score_ready, s + 1)
                for c in range(CHUNKS):
                    t = slice(c * CHUNK_TILES, (c + 1) * CHUNK_TILES)
                    if c >= 2:
                        dve.wait_ge(interest_done, s * CHUNKS + c - 1)
                    dve.tensor_tensor(z2_ps[:, c % 2, :].rearrange("p (t d) -> p t d", d=D),
                                      rows[:, par, t, :],
                                      score_ps[:, t].rearrange("p (t a) -> p t a", a=1
                                                               ).to_broadcast([P, CHUNK_TILES, D]),
                                      ALU.mult).then_inc(weighted, 1)
                    if c >= 1:
                        add_chunk(c - 1)
                add_chunk(CHUNKS - 1)
                dve.sem_inc(rows_free, 1)

            with dve.Fori(0, S // 2) as i:
                for par in range(2):
                    step(i, par)


def kernel(**inputs):
    from concourse import bacc
    from concourse.bass_utils import run_bass_kernel_spmd

    x = np.asarray(inputs["r_x"])
    batch, width = x.shape
    ids = np.zeros((width + LOOKAHEAD, P, batch // P), x.dtype)
    ids[:width] = x.T.reshape(width, P, batch // P)
    p = np.arange(P)
    arrays = {"ids": ids}
    for name in ("emb", "au_W1", "au_b1", "au_a1", "au_W2", "au_b2", "au_a2", "au_W3", "au_b3",
                 "mlp_W1", "mlp_b1", "mlp_W2", "mlp_b2", "mlp_W3", "mlp_b3"):
        arrays[name] = np.ascontiguousarray(inputs["L0_rec_" + name])
    h1, h2 = arrays["au_W2"].shape
    arrays["identity"] = np.eye(P, dtype=np.float32)
    arrays["same32"] = (p[:, None] % h1 == p[None, :] % h1).astype(np.float32) * np.float32(h1 / P)
    arrays["same16"] = (p[:, None] % h2 == p[None, :] % h2).astype(np.float32) * np.float32(h2 / P)

    nc = bacc.Bacc("TRN2", target_bir_lowering=False, num_devices=1)
    args = {n: nc.dram_tensor(n, a.shape, mybir.dt.from_np(a.dtype), kind="ExternalInput").ap()
            for n, a in arrays.items()}
    args["out"] = nc.dram_tensor("out", (P, batch // P), F32, kind="ExternalOutput").ap()
    din_kernel(nc, **args)
    got = run_bass_kernel_spmd(nc, [arrays], core_ids=[0])
    return got.results[0]["out"].reshape(batch)
```
